# Optimizing a Trainium2 kernel written in Bass

```python
import numpy as np
import jax
import jax.numpy as jnp

def _softmax(x, axis=-1):
    return jax.nn.softmax(x, axis=axis)

def _gelu(x):
    return jax.nn.gelu(x, approximate=True)

def _silu(x):
    return jax.nn.silu(x)

def _sigmoid(x):
    return jax.nn.sigmoid(x)

def _layernorm(x, axis=-1, eps=1e-05):
    m = jnp.mean(x, axis=axis, keepdims=True)
    v = jnp.var(x, axis=axis, keepdims=True)
    return (x - m) / jnp.sqrt(v + eps)

def _scatter_add(tgt, idx, src, axis=0):
    return tgt.at[idx].add(src)

def _segment_sum(src, seg, n):
    return jax.ops.segment_sum(src, seg, n)
kernel_name = 'mk_gnn_preln_d4_gnn_r32_c42d46'

def setup_inputs(seed: int=0):
    np.random.seed(seed)
    _w = jnp.asarray

    def _rec_inputs():
        import jax
        import jax.numpy as jnp
        _gk = jax.random.key(seed)
        x = -0.000202 + 1 * jax.random.normal(jax.random.fold_in(_gk, 1), (3125, 64), jnp.float32)
        _s = jax.random.randint(jax.random.fold_in(_gk, 2), (50000,), 0, 3125, jnp.int32)
        _d = jax.random.randint(jax.random.fold_in(_gk, 3), (50000,), 0, 3125, jnp.int32)
        _loop = jnp.arange(3125, dtype=jnp.int32)
        src = jnp.concatenate([_s, _d, _loop])
        dst = jnp.concatenate([_d, _s, _loop])
        _o = jnp.argsort(dst, stable=True)
        src = src[_o]
        dst = dst[_o]
        edge_attr_16 = -5.25733e-05 + 1.00007 * jax.random.normal(jax.random.fold_in(_gk, 12), (103125, 16), jnp.float32)
        return (x, src, dst, edge_attr_16)
    x, src, dst, edge_attr_16 = _rec_inputs()

    def _L0_gnn_setup():
        import jax, jax.numpy as jnp
        import numpy as np
        N_NODES = 3125
        N_EDGES = 37500
        IN_C, HID_C, OUT_C = (64, 64, 64)

        def _sage_conv(x, src, dst, Wl, b, Wr):
            msg = x[src]
            ssum = jax.ops.segment_sum(msg, dst, num_segments=N_NODES)
            cnt = jax.ops.segment_sum(jnp.ones((src.shape[0], 1), x.dtype), dst, num_segments=N_NODES)
            aggr = ssum / jnp.maximum(cnt, 1.0)
            return aggr @ Wl.T + b + x @ Wr.T
        key = jax.random.key(seed)
        ks = jax.random.split(key, 12)
        x = jax.random.normal(ks[0], (N_NODES, IN_C), dtype=jnp.float32)
        edge_index = jax.random.randint(ks[1], (2, N_EDGES), 0, N_NODES, dtype=jnp.int64)

        def lin(k, out_c, in_c):
            s = 1.0 / np.sqrt(in_c)
            return jax.random.uniform(k, (out_c, in_c), jnp.float32, -s, s)
        return {'x': x, 'edge_index': edge_index, 'W1l': lin(ks[2], HID_C, IN_C), 'b1': jnp.zeros((HID_C,), jnp.float32), 'W1r': lin(ks[3], HID_C, IN_C), 'W2l': lin(ks[4], HID_C, HID_C), 'b2': jnp.zeros((HID_C,), jnp.float32), 'W2r': lin(ks[5], HID_C, HID_C), 'W3l': lin(ks[6], OUT_C, HID_C), 'b3': jnp.zeros((OUT_C,), jnp.float32), 'W3r': lin(ks[7], OUT_C, HID_C)}
    _L0_gnn_all = _L0_gnn_setup()
    _L0_gnn_in = {k: v for k, v in _L0_gnn_all.items() if k in ('W1l', 'b1', 'W1r', 'W2l', 'b2', 'W2r', 'W3l', 'b3', 'W3r')}
    del _L0_gnn_all

    def _L1_gnn_setup():
        import jax, jax.numpy as jnp
        import numpy as np
        N = 3125
        E = 31250
        D = 64
        DE = 16
        BN_EPS = 1e-05
        key = jax.random.key(seed)
        ks = jax.random.split(key, 12)
        inp = {'node_feats': jax.random.normal(ks[0], (N, D), jnp.float32), 'edge_feats': jax.random.normal(ks[1], (E, DE), jnp.float32), 'src': jax.random.randint(ks[2], (E,), 0, N, jnp.int32), 'dst': jax.random.randint(ks[3], (E,), 0, N, jnp.int32), 'W_e': jax.random.normal(ks[4], (D, DE), jnp.float32) / np.sqrt(DE), 'b_e': jnp.zeros((D,), jnp.float32), 'eps': jnp.zeros((1,), jnp.float32), 'W1': jax.random.normal(ks[5], (2 * D, D), jnp.float32) / np.sqrt(D), 'b1': jnp.zeros((2 * D,), jnp.float32), 'gamma': jnp.ones((2 * D,), jnp.float32), 'beta': jnp.zeros((2 * D,), jnp.float32), 'W2': jax.random.normal(ks[6], (D, 2 * D), jnp.float32) / np.sqrt(2 * D), 'b2': jnp.zeros((D,), jnp.float32)}
        return inp
    _L1_gnn_all = _L1_gnn_setup()
    _L1_gnn_in = {k: v for k, v in _L1_gnn_all.items() if k in ('W_e', 'b_e', 'eps', 'W1', 'b1', 'gamma', 'beta', 'W2', 'b2')}
    del _L1_gnn_all

    def _L2_gnn_setup():
        import jax, jax.numpy as jnp
        import numpy as np
        N, E = (50000, 25000)
        NODE_DIM, EDGE_DIM, HEADS = (64, 16, 4)
        C = NODE_DIM // HEADS
        NEG_SLOPE = 0.2
        BN_EPS = 1e-05
        key = jax.random.key(seed)
        ks = jax.random.split(key, 12)
        glorot = lambda k, shape: jax.random.normal(k, shape, jnp.float32) * np.sqrt(2.0 / (shape[0] + shape[-1]))
        return {'x': jax.random.normal(ks[0], (N, NODE_DIM), jnp.float32), 'edge_index': jax.random.randint(ks[1], (2, E), 0, N, jnp.int32), 'edge_attr': jax.random.normal(ks[2], (E, EDGE_DIM), jnp.float32), 'W_l': glorot(ks[3], (NODE_DIM, HEADS * C)), 'b_l': jnp.zeros((HEADS * C,), jnp.float32), 'W_r': glorot(ks[4], (NODE_DIM, HEADS * C)), 'b_r': jnp.zeros((HEADS * C,), jnp.float32), 'W_e': glorot(ks[5], (EDGE_DIM, HEADS * C)), 'att': glorot(ks[6], (HEADS, C)), 'bias': jnp.zeros((HEADS * C,), jnp.float32), 'gamma': jnp.ones((NODE_DIM,), jnp.float32), 'beta': jnp.zeros((NODE_DIM,), jnp.float32)}
    _L2_gnn_all = _L2_gnn_setup()
    _L2_gnn_in = {k: v for k, v in _L2_gnn_all.items() if k in ('W_l', 'b_l', 'W_r', 'b_r', 'W_e', 'att', 'bias', 'gamma', 'beta')}
    del _L2_gnn_all

    def _L3_gnn_setup():
        import jax, jax.numpy as jnp
        import numpy as np
        NEG_SLOPE = 0.01
        key = jax.random.key(seed)
        k1, k2, k3, k4 = jax.random.split(key, 4)
        N, F, E = (50000, 64, 25000)
        h = jax.random.normal(k1, (N, F), dtype=jnp.float32)
        attn_w = jax.random.normal(k2, (2 * F,), dtype=jnp.float32) * (1.0 / np.sqrt(2 * F))
        src = jax.random.randint(k3, (E,), 0, N, dtype=jnp.int32)
        dst = jnp.sort(jax.random.randint(k4, (E,), 0, N, dtype=jnp.int32))
        return {'h': h, 'attn_w': attn_w, 'src': src, 'dst': dst}
    _L3_gnn_all = _L3_gnn_setup()
    _L3_gnn_in = {k: v for k, v in _L3_gnn_all.items() if k in ('attn_w',)}
    del _L3_gnn_all
    return {'x': x, 'src': src, 'dst': dst, 'edge_attr_16': edge_attr_16, 'L0_gnn_W1l': _L0_gnn_in['W1l'], 'L0_gnn_b1': _L0_gnn_in['b1'], 'L0_gnn_W1r': _L0_gnn_in['W1r'], 'L0_gnn_W2l': _L0_gnn_in['W2l'], 'L0_gnn_b2': _L0_gnn_in['b2'], 'L0_gnn_W2r': _L0_gnn_in['W2r'], 'L0_gnn_W3l': _L0_gnn_in['W3l'], 'L0_gnn_b3': _L0_gnn_in['b3'], 'L0_gnn_W3r': _L0_gnn_in['W3r'], 'L1_gnn_W_e': _L1_gnn_in['W_e'], 'L1_gnn_b_e': _L1_gnn_in['b_e'], 'L1_gnn_eps': _L1_gnn_in['eps'], 'L1_gnn_W1': _L1_gnn_in['W1'], 'L1_gnn_b1': _L1_gnn_in['b1'], 'L1_gnn_gamma': _L1_gnn_in['gamma'], 'L1_gnn_beta': _L1_gnn_in['beta'], 'L1_gnn_W2': _L1_gnn_in['W2'], 'L1_gnn_b2': _L1_gnn_in['b2'], 'L2_gnn_W_l': _L2_gnn_in['W_l'], 'L2_gnn_b_l': _L2_gnn_in['b_l'], 'L2_gnn_W_r': _L2_gnn_in['W_r'], 'L2_gnn_b_r': _L2_gnn_in['b_r'], 'L2_gnn_W_e': _L2_gnn_in['W_e'], 'L2_gnn_att': _L2_gnn_in['att'], 'L2_gnn_bias': _L2_gnn_in['bias'], 'L2_gnn_gamma': _L2_gnn_in['gamma'], 'L2_gnn_beta': _L2_gnn_in['beta'], 'L3_gnn_attn_w': _L3_gnn_in['attn_w']}

def reference(x, src, dst, edge_attr_16, L0_gnn_W1l, L0_gnn_b1, L0_gnn_W1r, L0_gnn_W2l, L0_gnn_b2, L0_gnn_W2r, L0_gnn_W3l, L0_gnn_b3, L0_gnn_W3r, L1_gnn_W_e, L1_gnn_b_e, L1_gnn_eps, L1_gnn_W1, L1_gnn_b1, L1_gnn_gamma, L1_gnn_beta, L1_gnn_W2, L1_gnn_b2, L2_gnn_W_l, L2_gnn_b_l, L2_gnn_W_r, L2_gnn_b_r, L2_gnn_W_e, L2_gnn_att, L2_gnn_bias, L2_gnn_gamma, L2_gnn_beta, L3_gnn_attn_w):
    import jax
    import jax.numpy as jnp

    def _L0_gnn_ref(x, edge_index, W1l, b1, W1r, W2l, b2, W2r, W3l, b3, W3r):
        import jax, jax.numpy as jnp
        import numpy as np
        N_NODES = 3125
        N_EDGES = 37500
        IN_C, HID_C, OUT_C = (64, 64, 64)

        def _sage_conv(x, src, dst, Wl, b, Wr):
            msg = x[src]
            ssum = jax.ops.segment_sum(msg, dst, num_segments=N_NODES)
            cnt = jax.ops.segment_sum(jnp.ones((src.shape[0], 1), x.dtype), dst, num_segments=N_NODES)
            aggr = ssum / jnp.maximum(cnt, 1.0)
            return aggr @ Wl.T + b + x @ Wr.T
        src, dst = (edge_index[0], edge_index[1])
        h = jax.nn.relu(_sage_conv(x, src, dst, W1l, b1, W1r))
        h = jax.nn.relu(_sage_conv(h, src, dst, W2l, b2, W2r))
        return _sage_conv(h, src, dst, W3l, b3, W3r)

    def _L1_gnn_ref(node_feats, edge_feats, src, dst, W_e, b_e, eps, W1, b1, gamma, beta, W2, b2):
        import jax, jax.numpy as jnp
        import numpy as np
        N = 3125
        E = 31250
        D = 64
        DE = 16
        BN_EPS = 1e-05
        ef = edge_feats @ W_e.T + b_e
        m = jax.nn.relu(ef + node_feats[src])
        agg = jax.ops.segment_sum(m, dst, num_segments=N)
        h = agg + (1.0 + eps) * node_feats
        h1 = h @ W1.T + b1
        mu = jnp.mean(h1, axis=0)
        var = jnp.mean((h1 - mu) ** 2, axis=0)
        h1 = (h1 - mu) * jax.lax.rsqrt(var + BN_EPS) * gamma + beta
        h1 = jax.nn.relu(h1)
        return h1 @ W2.T + b2

    def _L2_gnn_ref(x, edge_index, edge_attr, W_l, b_l, W_r, b_r, W_e, att, bias, gamma, beta):
        import jax, jax.numpy as jnp
        import numpy as np
        N, E = (50000, 25000)
        NODE_DIM, EDGE_DIM, HEADS = (64, 16, 4)
        C = NODE_DIM // HEADS
        NEG_SLOPE = 0.2
        BN_EPS = 1e-05
        src, dst = (edge_index[0], edge_index[1])
        n = x.shape[0]
        xl = (x @ W_l + b_l).reshape(n, HEADS, C)
        xr = (x @ W_r + b_r).reshape(n, HEADS, C)
        e = (edge_attr @ W_e).reshape(-1, HEADS, C)
        g = jax.nn.leaky_relu(xl[src] + xr[dst] + e, NEG_SLOPE)
        logits = jnp.einsum('ehc,hc->eh', g, att)
        amax = jax.ops.segment_max(logits, dst, num_segments=n)
        ex = jnp.exp(logits - amax[dst])
        denom = jax.ops.segment_sum(ex, dst, num_segments=n)
        alpha = ex / (denom[dst] + 1e-16)
        msg = xl[src] * alpha[..., None]
        out = jax.ops.segment_sum(msg, dst, num_segments=n).reshape(n, HEADS * C) + bias
        mean = out.mean(axis=0)
        var = out.var(axis=0)
        out = (out - mean) * jax.lax.rsqrt(var + BN_EPS) * gamma + beta
        return jax.nn.gelu(out + x, approximate=False)

    def _L3_gnn_ref(h, attn_w, src, dst):
        import jax, jax.numpy as jnp
        import numpy as np
        NEG_SLOPE = 0.01
        N, F = h.shape
        z_src = h[src]
        z_dst = h[dst]
        e = z_src @ attn_w[:F] + z_dst @ attn_w[F:]
        e = jnp.where(e >= 0, e, NEG_SLOPE * e)
        e_max = jax.ops.segment_max(e, dst, num_segments=N)
        e_exp = jnp.exp(e - e_max[dst])
        denom = jax.ops.segment_sum(e_exp, dst, num_segments=N)
        alpha = e_exp / denom[dst]
        out = jax.ops.segment_sum(alpha[:, None] * z_src, dst, num_segments=N)
        return out
    edge_index = jnp.stack([src, dst])
    h = jnp.maximum(_layernorm(x, axis=-1), 0.0)
    x = x + _L0_gnn_ref(h, edge_index, L0_gnn_W1l, L0_gnn_b1, L0_gnn_W1r, L0_gnn_W2l, L0_gnn_b2, L0_gnn_W2r, L0_gnn_W3l, L0_gnn_b3, L0_gnn_W3r)
    h = jnp.maximum(_layernorm(x, axis=-1), 0.0)
    x = x + _L1_gnn_ref(h, edge_attr_16, src, dst, L1_gnn_W_e, L1_gnn_b_e, L1_gnn_eps, L1_gnn_W1, L1_gnn_b1, L1_gnn_gamma, L1_gnn_beta, L1_gnn_W2, L1_gnn_b2)
    h = jnp.maximum(_layernorm(x, axis=-1), 0.0)
    x = x + _L2_gnn_ref(h, edge_index, edge_attr_16, L2_gnn_W_l, L2_gnn_b_l, L2_gnn_W_r, L2_gnn_b_r, L2_gnn_W_e, L2_gnn_att, L2_gnn_bias, L2_gnn_gamma, L2_gnn_beta)
    h = jnp.maximum(_layernorm(x, axis=-1), 0.0)
    x = x + _L3_gnn_ref(h, L3_gnn_attn_w, src, dst)
    return x

_drawn_inputs = setup_inputs


def setup_inputs(seed=0):
    import zlib

    import numpy as np

    out = dict(_drawn_inputs(seed))
    spreads = {'L0_gnn_b1': (0.0, 0.316),
     'L0_gnn_b2': (0.0, 0.1),
     'L0_gnn_b3': (0.0, 0.1),
     'L1_gnn_b_e': (0.0, 0.1),
     'L1_gnn_b1': (0.0, 0.8),
     'L1_gnn_gamma': (1.0, 0.2),
     'L1_gnn_beta': (0.0, 0.1),
     'L1_gnn_b2': (0.0, 0.1),
     'L2_gnn_b_l': (0.0, 0.493),
     'L2_gnn_b_r': (0.0, 0.602),
     'L2_gnn_bias': (0.0, 0.8),
     'L2_gnn_gamma': (1.0, 0.2),
     'L2_gnn_beta': (0.0, 0.1)}
    factors = {'L3_gnn_attn_w': 8.0}
    for name, (base, spread) in spreads.items():
        noise = np.random.default_rng([zlib.crc32(name.encode()), seed]).standard_normal(out[name].shape)
        drawn = base * np.exp(spread * noise) if base else spread * noise
        out[name] = jnp.asarray(drawn.astype(out[name].dtype))
    for name, factor in factors.items():
        out[name] = (out[name] * factor).astype(out[name].dtype)
    return out
```

```python
from contextlib import ExitStack

import concourse.bass as bass
from concourse import mybir

F32 = mybir.dt.float32
I32 = mybir.dt.int32
ALU = mybir.AluOpType
ACT = mybir.ActivationFunctionType
AX_X = mybir.AxisListType.X
PE_ENGINE = mybir.EngineType.PE
SP_ENGINE = mybir.EngineType.SP

P = 128
N, E, D, DE, HEADS = 3125, 103125, 64, 16, 4
D2 = 2 * D
NB = -(-N // P)
NPAD = NB * P
TAIL = N - (NB - 1) * P
NT = -(-E // P)
G, RING = 4, 4
BODY = G * RING
NQ = -(-(NT + NB - 1) // BODY) * BODY
ITERS = NQ // BODY
QB = -(-NQ // P) + (1 if NQ % P == 0 else 0)
QPAD = QB * P
HALO = P + 2
W = D + HEADS
PER_BANK = 512 // W
PASSES = 6
BIG = 1.0e38
EPS = 1e-5
GROUPS = [(4 * g, min(4, NB - 4 * g)) for g in range(-(-NB // 4))]
BANKS = [(k, PER_BANK * k, min(PER_BANK, NB - PER_BANK * k)) for k in range(-(-NB // PER_BANK))]


def build(nc, x, src_flat, dst_flat, attr_t, w_sage, b_sage, we1, w1t, b1, gamma1, beta1, eps1, w2t, b2,
          wlr, we2, att, bias2, gamma2, beta2, attn, out):
    with ExitStack() as ctx:
        def sb(name, shape, dt=F32):
            return ctx.enter_context(nc.sbuf_tensor(name, shape, dt))

        def sem(name):
            return ctx.enter_context(nc.semaphore(name))

        def dram(name, shape, dt=F32):
            return nc.dram_tensor(name, shape, dt, kind="Internal")

        halo_d = dram("halo_d", (NT, HALO), I32)
        pair_rows_d = dram("pair_rows_d", (4, QPAD), I32)
        flags_d = dram("flags_d", (4, QPAD * P))
        tables = [dram(f"table{p}", (NPAD, D)) for p in range(PASSES)]
        gathered_d = [dram(f"gathered{p}_d", (P, NQ, D)) for p in (4, 5)]
        logit_d = [dram(f"logit{p}_d", (h, QPAD * P)) for p, h in ((4, HEADS), (5, 1))]
        weight_d = [dram(f"weight{p}_d", (h, QPAD * P)) for p, h in ((4, HEADS), (5, 1))]

        X = sb("X", [P, NB, D])
        C = sb("C", [P, NB, D2])
        CZ = sb("CZ", [P, 2 * NPAD])
        CT = CZ[:, 0:NPAD]
        ZT = CZ[:, NPAD:2 * NPAD]
        wk = CZ[:, 0:6 * QB * P].rearrange("p (k j e) -> p k j e", k=6, e=P)
        HT = sb("HT", [P, NPAD])
        XR = sb("XR", [P, NB + 1, D])
        AD = sb("AD", [P, NB + 1])
        st = sb("st", [P, 8, NB])
        bn = sb("bn", [P, 12])
        src_i = sb("src_i", [P, QPAD], I32)
        dloc = sb("dloc", [P, QPAD])
        rows = sb("rows", [1, 4, QPAD], I32)
        idx = sb("idx", [P, BODY], I32)
        GB = sb("GB", [P, BODY, W])
        OH = sb("OH", [P, BODY, P])
        OT = sb("OT", [P, RING, G * P])
        MS = sb("MS", [P, BODY, W])
        MR = sb("MR", [P, BODY, W])
        AT = sb("AT", [DE + 1, BODY * P])
        LG = sb("LG", [P, QPAD, HEADS])
        tq = sb("tq", [P, HEADS, P * 2])
        flags = sb("flags", [P, 4, NQ])
        V = sb("V", [P, NQ])
        FW = sb("FW", [P, NQ])
        BW = sb("BW", [P, NQ])
        car = sb("car", [P, 4])
        crow = sb("crow", [1, 4, P])
        iota_i = sb("iota_i", [P, NQ], I32)
        iota_f = sb("iota_f", [P, NQ])
        part_i = sb("part_i", [P, QB], I32)
        part_f = sb("part_f", [P, QB])
        ident = sb("ident", [P, P])
        ones = sb("ones", [1, P])
        edge_i = sb("edge_i", [1, 2, NT], I32)
        edge_f = sb("edge_f", [1, 4, NT])
        CD = OH[:, :, :].rearrange("p a b -> p (a b)")[:, 0:2 * NT].rearrange("p (k t) -> p k t", k=2)
        pq = sb("pq", [P, 12, QB])
        pqi = sb("pqi", [P, 5, QB], I32)
        hg = sb("hg", [P, QB, HALO], I32)
        hf = sb("hf", [P, QB, HALO])
        sg = sb("sg", [P, QB, P], I32)
        wsage = sb("wsage", [P, 3, D])
        bsage = sb("bsage", [D, 3])
        we1s = sb("we1s", [DE + 1, D])
        w1s = sb("w1s", [D, D2])
        v1s = sb("v1s", [P, 3])
        eps_s = sb("eps_s", [P, 1])
        w2s = sb("w2s", [P, D])
        v2s = sb("v2s", [D, 4])
        wlrs = sb("wlrs", [D + 1, D2])
        we2s = sb("we2s", [DE, D])
        att_s = sb("att_s", [P, D])
        attn_s = sb("attn_s", [P, D2])

        ps = ctx.enter_context(nc.psum_tensor("ps", [P, 8, 512], F32))
        psf = ps[:, :, :].rearrange("p a b -> p (a b)")

        names = ["x_loaded", "weights_loaded", "halo_made", "edges_loaded", "iota_made", "ident_made",
                 "pool_const", "edge_rows", "edge_bc", "cd_copied", "pair_tile", "rows_stored", "rows_loaded",
                 "halo_gathered", "flags_ready", "flags_stored", "flags_loaded", "pt", "pt_copied",
                 "sqrt_in", "sqrt_out", "consts_set"]
        S = {n: sem(n) for n in names}

        class Own:
            def __init__(self, eng, s):
                self.eng, self.s, self.n = eng, s, 0

            def __call__(self, ins):
                self.n += 1
                ins.then_inc(self.s, 1)
                self.eng.wait_ge(self.s, self.n)
        own_dve, own_act = sem("own_dve"), sem("own_act")
        sqrt_no = [0]

        SHARED = ("staged", "gathered", "attr", "xg_stored", "xg_loaded", "table_ready", "table_stored", "sums_zeroed",
                  "sums_done", "slot_free", "onehot_ready", "tr", "tr_read", "mm", "mm_read", "bk", "bk_read")
        STAGES = {"tr": ["n0", "n1", "n2", "n3a", "n4a", "n4b"], "mm": ["n0", "n1", "n2", "n3a", "n3b", "n4a"],
                  "bk": ["n0", "n1", "n2", "n3b", "n4b"]}

        def gone(kind, s_):
            return len(GROUPS) * STAGES[kind].index(s_)

        class Named(dict):
            def __missing__(self, key):
                if key[0] in SHARED:
                    name = "_".join(map(str, key[:1] + key[2:]))
                    if name not in ring_sems:
                        ring_sems[name] = sem(name)
                    self[key] = ring_sems[name]
                else:
                    self[key] = sem("_".join(map(str, key)))
                return self[key]
        ring_sems = {}
        K, T = Named(), Named()
        for n in ["attr_free3", "ef_ready3", "ef_free3", "sum_ready3", "msg_ready3", "msg_free3"]:
            K[n] = sem(n)
        batches_begun = sem("batches_begun")
        sp_went_on = sem("sp_went_on")
        bn_in, bn_out = sem("bn_in"), sem("bn_out")
        out_stored = sem("out_stored")

        ctx.enter_context(nc.allow_non_contiguous_dma(reason="a few hundred single numbers, once"))
        block = ctx.enter_context(nc.Block())

        def acc_view(k, nb):
            return ps[:, k, 0:nb * W].rearrange("p (b w) -> p b w", w=W)

        def loads(engine, row, q0):
            top = [3 * 512 + (PER_BANK - 1) * W, NB * D, (NT - 1) * P, NB][row]
            return nc.values_load_multi_w_load_instructions(
                rows[0:1, row, bass.ds(q0, G)], engines=[engine], min_val=0, max_val=top,
                skip_runtime_bounds_check_because="clamped on the chip when the rows are made")[1]

        @block.sync
        def _(sp):
            sp.dma_start(halo_d[:, :], bass.AP(dst_flat.tensor, 0, [[P, NT], [1, HALO]])).then_inc(S["halo_made"], 16)
            for k, at in enumerate((1, P)):
                sp.dma_start(edge_i[0:1, k, :], bass.AP(dst_flat.tensor, at, [[P * NT, 1], [P, NT]])).then_inc(S["edges_loaded"], 16)
            sp.wait_ge(S["consts_set"], 1)
            sp.dma_start(X[:, 0:NB - 1, :], x[0:(NB - 1) * P, :].rearrange("(b p) d -> p b d", p=P)).then_inc(S["x_loaded"], 16)
            sp.dma_start(X[0:TAIL, NB - 1, :], x[(NB - 1) * P:N, :]).then_inc(S["x_loaded"], 16)
            for dst_, src_ in ((wsage[:, :, :], w_sage.rearrange("l k n -> k l n")), (bsage[:, :], b_sage), (we1s[:, :], we1),
                               (w1s[:, :], w1t), (v1s[:, 0:1], b1), (v1s[:, 1:2], gamma1), (v1s[:, 2:3], beta1),
                               (eps_s[:, :], eps1.partition_broadcast(P)), (w2s[:, :], w2t), (v2s[:, 0:1], b2),
                               (v2s[:, 1:2], bias2), (v2s[:, 2:3], gamma2), (v2s[:, 3:4], beta2), (wlrs[:, :], wlr),
                               (we2s[:, :], we2), (att_s[:, :], att.partition_broadcast(P)),
                               (attn_s[:, :], attn.partition_broadcast(P))):
                sp.dma_start(dst_, src_).then_inc(S["weights_loaded"], 16)

            sp.wait_ge(S["pair_tile"], 1)
            sp.dma_start(pair_rows_d[:, :].rearrange("r (j p) -> p r j", p=P), pqi[:, 0:4, :]).then_inc(S["rows_stored"], 16)
            sp.wait_ge(S["rows_stored"], 16)
            sp.dma_start(rows[0:1, :, :], bass.AP(pair_rows_d, 0, [[4 * QPAD, 1], [QPAD, 4], [1, QPAD]])).then_inc(S["rows_loaded"], 16)
            sp.wait_ge(S["flags_ready"], 1)
            for f in range(4):
                sp.dma_start(flags_d[f, :].rearrange("(j p e) -> p j e", p=P, e=P), wk[:, f, :, :]).then_inc(S["flags_stored"], 16)
            sp.wait_ge(S["flags_stored"], 64)
            for f in range(4):
                sp.dma_start(flags[:, f, :], flags_d[f, 0:P * NQ].rearrange("(r s) -> r s", r=P)).then_inc(S["flags_loaded"], 16)

            def store_table(p, cols):
                sp.wait_ge(K["table_ready", p], p + 1)
                sp.dma_start(tables[p][:, 0:D].rearrange("(b c) d -> c b d", c=P), cols[:, :, :]).then_inc(K["table_stored", p], 16)

            def stage(p, n, r):
                q0 = sp.snap(n * G)
                free, stored = sp.snap(n + 1 + p * (RING + ITERS * RING)), sp.snap(n + 1)
                sp.wait_ge(K["slot_free", p], free)
                if p >= 4:
                    sp.sem_inc(sp_went_on, 1)
                    sp.wait_ge(K["store_free", p], stored)
                sp.dma_start(idx[:, G * r:G * r + G], src_i[:, bass.ds(q0, G)]).then_inc(K["staged", p, r], 16)

            def load_attr(p, n, r):
                cols = loads(SP_ENGINE, 2, n * G)
                if p == 3:
                    free = sp.snap(n + 1)
                    sp.wait_ge(K["attr_free3"], free)
                    sp.sem_inc(sp_went_on, 1)
                for j, col in enumerate(cols):
                    at = (G * r + j) * P
                    sp.dma_start(AT[0:DE, at:at + P], attr_t[:, bass.ds(col, P)]).then_inc(K["attr", p, r], 16)

            def gather_pass(p):
                with sp.Fori(0, ITERS) as i:
                    for r in range(RING):
                        stage(p, i * RING + r, r)
                        if p in (3, 4):
                            load_attr(p, i * RING + r, r)

            for p in range(3):
                store_table(p, C[:, :, D:D2])
                if p == 0:
                    sp.wait_ge(S["rows_loaded"], 16)
                    sp.wait_ge(S["pt_copied"], 2 * QB)
                gather_pass(p)
            store_table(3, C[:, :, D:D2])
            gather_pass(3)
            store_table(4, C[:, :, 0:D])

            def relayout_and_weigh(p, H, k):
                for j in range(QB):
                    sp.wait_ge(K["lt_copied", p], j + 1)
                    sp.dma_start(logit_d[k][:, j * P * P:(j + 1) * P * P].rearrange("h (q e) -> q h e", e=P),
                                 tq[:, 0:H, (j % 2) * P:(j % 2 + 1) * P]).then_inc(K["lt_stored", p, j % 2], 16)
                for half in range(2):
                    sp.wait_ge(K["lt_stored", p, half], 16 * len(range(half, QB, 2)))
                for h in range(H):
                    if h:
                        sp.wait_ge(K["scan_done", p], h)
                    sp.dma_start(V[:, :], logit_d[k][h, 0:P * NQ].rearrange("(r s) -> r s", r=P)).then_inc(K["lt_loaded", p], 16)
                    sp.wait_ge(K["ex_done", p], h + 1)
                    sp.dma_start(weight_d[k][h, 0:P * NQ].rearrange("(r s) -> r s", r=P), FW[:, :]).then_inc(K["wt_stored", p], 16)
                sp.wait_ge(K["wt_stored", p], 16 * H)
                for j in range(QB):
                    n = min(P, NQ - j * P)
                    if j >= 2:
                        sp.wait_ge(K["wt_copied", p], j - 1)
                    sp.dma_start(tq[0:n, 0:H, (j % 2) * P:(j % 2 + 1) * P],
                                 weight_d[k][:, j * P * P:j * P * P + n * P].rearrange("h (q e) -> q h e", e=P)).then_inc(K["wt_loaded", p, j % 2], 16)

            def weighted_sums(p, k):
                sp.wait_ge(K["store_free", p], RING + ITERS * RING)
                with sp.Fori(0, ITERS) as i:
                    for r in range(RING):
                        q0 = sp.snap((i * RING + r) * G)
                        sp.wait_ge(K["b_free", p], i * RING + r + 1)
                        sp.dma_start(GB[:, G * r:G * r + G, 0:D], gathered_d[k][:, bass.ds(q0, G), :]).then_inc(K["xg_loaded", p, r], 16)

            gather_pass(4)
            relayout_and_weigh(4, HEADS, 0)
            weighted_sums(4, 0)
            sp.wait_ge(K["table_ready", 5], 6)
            sp.dma_start(tables[5][:, 0:D].rearrange("(b c) d -> c b d", c=P), C[:, :, D:D2]).then_inc(K["table_stored", 5], 16)
            gather_pass(5)
            relayout_and_weigh(5, 1, 1)
            weighted_sums(5, 1)
            sp.wait_ge(bn_in, 3)
            sp.dma_start(out[0:(NB - 1) * P, :].rearrange("(b p) d -> p b d", p=P), X[:, 0:NB - 1, :]).then_inc(out_stored, 16)
            sp.dma_start(out[(NB - 1) * P:N, :], X[0:TAIL, NB - 1, :]).then_inc(out_stored, 16)
            sp.wait_ge(out_stored, 32)

        @block.gpsimd
        def _(pool):
            pool.iota(iota_i[:, :], [[1, NQ]], base=0, channel_multiplier=0)
            pool.iota(part_i[:, :], [[P, QB]], base=0, channel_multiplier=1).then_inc(S["iota_made"], 1)
            pool.wait_ge(S["pair_tile"], 1)
            pool.wait_ge(S["halo_made"], 16)
            for j in range(QB):
                at = bass.IndirectOffsetOnAxis(ap=pqi[:, 4, j:j + 1], axis=0)
                pool.indirect_dma_start(hg[:, j, :], None, halo_d[:, :], at).then_inc(S["halo_gathered"], 16)
                pool.indirect_dma_start(sg[:, j, :], None, src_flat.rearrange("(t e) -> t e", e=P), at).then_inc(S["halo_gathered"], 16)
            for p in range(PASSES):
                pool.wait_ge(K["table_stored", p], 16 * p + 16)
                with pool.Fori(0, ITERS) as i:
                    for r in range(RING):
                        pool.wait_ge(K["staged", p, r], 16 * i + 16 + 16 * ITERS * p)
                        pool.sem_inc(batches_begun, 1)
                        for j in range(G):
                            s = G * r + j
                            pool.indirect_dma_start(GB[:, s, 0:D], None, tables[p][:, 0:D],
                                                    bass.IndirectOffsetOnAxis(ap=idx[:, s:s + 1], axis=0)).then_inc(K["gathered", p, r], 16)

        @block.tensor
        def _(pe):
            def transposes(s_, C_in, src_of, wait_in):
                for g, (b0, nb) in enumerate(GROUPS):
                    pe.wait_ge(T["in_ready", s_], wait_in(g))
                    if g >= 2:
                        pe.wait_ge(T["tr_read", s_], g - 1 + gone("tr", s_))
                    for j in range(nb):
                        ins = nc.tensor.transpose(ps[0:C_in, 4 + g % 2, j * P:(j + 1) * P], src_of(b0 + j), ident[:, :])
                    ins.then_inc(T["tr", s_], 1)

            def products(s_, rows_out, lhsT, rhs, ready, ready_from=0):
                for g, (b0, nb) in enumerate(GROUPS):
                    pe.wait_ge(ready, g + 1 + ready_from)
                    if g >= 2:
                        pe.wait_ge(T["mm_read", s_], g - 1 + gone("mm", s_))
                    nc.tensor.matmul(ps[0:rows_out, 6 + g % 2, 0:nb * P], lhsT, rhs(b0 * P, (b0 + nb) * P),
                                     start=True, stop=True).then_inc(T["mm", s_], 1)

            def back(s_, C_in, src_of, ready, ready_from=0):
                for g, (b0, nb) in enumerate(GROUPS):
                    pe.wait_ge(ready, g + 1 + ready_from)
                    if g >= 2:
                        pe.wait_ge(T["bk_read", s_], g - 1 + gone("bk", s_))
                    for j in range(nb):
                        ins = nc.tensor.transpose(ps[:, g % 2, j * D:j * D + C_in], src_of((b0 + j) * P, (b0 + j + 1) * P),
                                                  ident[0:C_in, 0:C_in])
                    ins.then_inc(T["bk", s_], 1)

            def add_up(p, n, r, moving, width, free):
                for j, col in enumerate(loads(PE_ENGINE, 0, n * G)):
                    ins = nc.tensor.matmul(psf[:, bass.ds(col, width)], OH[:, G * r + j, :], moving[:, G * r + j, 0:width],
                                           start=False, stop=False, skip_group_check=True)
                ins.then_inc(free, 1)

            pe.wait_ge(S["ident_made"], 1)
            pe.wait_ge(S["edge_rows"], 1)
            for k in range(2):
                for c in range(2):
                    a, b = c * 512, min(NT, c * 512 + 512)
                    ins = nc.tensor.matmul(ps[:, 2 * k + c, 0:b - a], ones[0:1, :], edge_f[0:1, 2 + k, a:b], start=True, stop=True)
            ins.then_inc(S["edge_bc"], 1)
            pe.wait_ge(S["flags_ready"], 1)
            pe.wait_ge(S["cd_copied"], 1)
            for k in range(2):
                for j in range(QB):
                    n = k * QB + j
                    if n >= 4:
                        pe.wait_ge(S["pt_copied"], n - 3)
                    nc.tensor.transpose(ps[:, 4 + n % 4, 0:P], wk[:, 4 + k, j, :], ident[:, :]).then_inc(S["pt"], 1)

            pe.wait_ge(S["rows_loaded"], 16)
            pe.wait_ge(S["pt_copied"], 2 * QB)
            for p in range(3):
                pe.wait_ge(K["sums_zeroed", p], p + 1)
                with pe.Fori(0, ITERS) as i:
                    for r in range(RING):
                        pe.wait_ge(K["gathered", p, r], 16 * G * i + 16 * G + 16 * G * ITERS * p)
                        pe.wait_ge(K["onehot_ready", p], i * RING + r + 1 + p * ITERS * RING)
                        add_up(p, i * RING + r, r, GB, D + (p == 0), K["slot_free", p])
                nc.tensor.transpose(ps[:, 5, 0:P], ident[:, :], ident[:, :]).then_inc(K["sums_done", p], 1)
                s_ = f"n{p}"
                transposes(s_, P, lambda b: C[:, b, :], lambda g: 1)
                if p == 0:
                    pe.wait_ge(S["weights_loaded"], 16 * 17)
                products(s_, D, wsage[:, p, :], lambda a, b: CT[:, a:b], T["tr_read", s_], gone("tr", s_))
                back(s_, D, lambda a, b: HT[0:D, a:b], T["mm_read", s_], gone("mm", s_))

            p = 3
            def edge_terms3(n, r, i1):
                pe.wait_ge(K["attr", 3, r], 16 * G * i1)
                pe.wait_ge(K["ef_free3"], n + 1)
                for j in range(G):
                    ins = nc.tensor.matmul(ps[:, 4 + r, j * D:(j + 1) * D], AT[:, (G * r + j) * P:(G * r + j + 1) * P],
                                           we1s[:, :], start=True, stop=True)
                ins.then_inc(K["ef_ready3"], 1)
            pe.wait_ge(K["sums_zeroed", p], p + 1)
            with pe.Fori(0, ITERS) as i:
                for r in range(RING):
                    n = i * RING + r
                    edge_terms3(n, r, i + 1)
                    pe.wait_ge(K["onehot_ready", p], n + 1 + p * ITERS * RING)
                    pe.wait_ge(K["msg_ready3"], n + 1)
                    add_up(p, n, r, MR, D, K["onehot_free", p])
            nc.tensor.transpose(ps[:, 5, 0:P], ident[:, :], ident[:, :]).then_inc(K["sums_done", p], 1)
            transposes("n3a", D, lambda b: C[:, b, 0:D], lambda g: 1)
            products("n3a", P, w1s[:, :], lambda a, b: CT[0:D, a:b], T["tr_read", "n3a"], gone("tr", "n3a"))
            pe.wait_ge(bn_out, 1)
            products("n3b", D, w2s[:, :], lambda a, b: ZT[:, a:b], T["in_ready", "n3b"])
            back("n3b", D, lambda a, b: HT[0:D, a:b], T["mm_read", "n3b"], gone("mm", "n3b"))

            transposes("n4a", D, lambda b: C[:, b, D:D2], lambda g: 1)
            for g, (b0, nb) in enumerate(GROUPS):
                pe.wait_ge(T["tr_read", "n4a"], g + 1 + gone("tr", "n4a"))
                if g >= 2:
                    pe.wait_ge(T["mm_read", "n4a"], g - 1 + gone("mm", "n4a"))
                for j in range(nb):
                    ins = nc.tensor.matmul(ps[:, 6 + g % 2, j * P:(j + 1) * P], HT[0:D + 1, (b0 + j) * P:(b0 + j + 1) * P],
                                           wlrs[:, :], start=True, stop=True)
                ins.then_inc(T["mm", "n4a"], 1)

            def logits_pass(p):
                col_row = 1 if p == 4 else 3

                def turn(n, r):
                    pe.wait_ge(K["onehot_ready", p], n + 1 + p * ITERS * RING)
                    for j in range(G):
                        ins = nc.tensor.transpose(ps[:, r, j * P:(j + 1) * P], OH[:, G * r + j, :], ident[:, :])
                    ins.then_inc(K["tr_ready", p], 1)

                def terms(n, r, i):
                    cols = loads(PE_ENGINE, col_row, n * G)
                    if p == 4:
                        pe.wait_ge(K["attr", 4, r], 16 * G * i + 16 * G + 16 * G * ITERS)
                    pe.wait_ge(K["ot_ready", p], n + 1)
                    for j, col in enumerate(cols):
                        ot = OT[:, r, j * P:(j + 1) * P]
                        if p == 4:
                            nc.tensor.matmul(ps[:, 4 + r, j * D:(j + 1) * D], AT[0:DE, (G * r + j) * P:(G * r + j + 1) * P],
                                             we2s[:, :], start=True, stop=False)
                            ins = nc.tensor.matmul(ps[:, 4 + r, j * D:(j + 1) * D], ot,
                                                   XR[:, :, :].rearrange("p b d -> p (b d)")[:, bass.ds(col, D)],
                                                   start=False, stop=True)
                        else:
                            ins = nc.tensor.matmul(ps[:, 4 + r, j:j + 1], ot, AD[:, bass.ds(col, 1)], start=True, stop=True)
                    ins.then_inc(K["g_ready", p], 1)

                turn(0, 0)
                with pe.Fori(0, ITERS - 1) as i:
                    for r in range(RING):
                        turn(i * RING + r + 1, (r + 1) % RING)
                        terms(i * RING + r, r, i)
                for r in range(RING):
                    n = (ITERS - 1) * RING + r
                    if r + 1 < RING:
                        turn(n + 1, r + 1)
                    terms(n, r, ITERS - 1)

            def relayout(p, H):
                pe.wait_ge(K["logits_done", p], 1)
                for j in range(QB):
                    if j >= 2:
                        pe.wait_ge(K["lt_copied", p], j - 1)
                    for h in range(H):
                        ins = nc.tensor.transpose(ps[:, j % 2, h * P:(h + 1) * P], LG[:, j * P:(j + 1) * P, h], ident[:, :])
                    ins.then_inc(K["lt", p], 1)
                for h in range(H):
                    for d in range(2):
                        n = 2 * h + d
                        pe.wait_ge(K["carry_t", p], n + 1)
                        nc.tensor.transpose(ps[0:1, 2, 0:P], car[:, 0:1], ident[:, :])
                        nc.tensor.transpose(ps[0:1, 2, P:2 * P], car[:, 1:2], ident[:, :]).then_inc(K["carry_row", p], 1)
                        pe.wait_ge(K["carry_t", p], n + 1)
                        pe.wait_ge(K["carry_back", p], 2 * n + 1)
                        nc.tensor.transpose(ps[:, 3, 0:1], crow[0:1, 1, :], ident[0:1, 0:1]).then_inc(K["carry_row", p], 1)
                        pe.wait_ge(K["carry_back", p], 2 * n + 2)
                for j in range(QB):
                    m = min(P, NQ - j * P)
                    pe.wait_ge(K["wt_loaded", p, j % 2], 16 * (j // 2) + 16)
                    if j >= 2:
                        pe.wait_ge(K["wt_copied", p], j - 1)
                    for h in range(H):
                        ins = nc.tensor.transpose(ps[:, j % 2, h * P:h * P + m], tq[0:m, h, (j % 2) * P:(j % 2 + 1) * P], ident[0:m, 0:m])
                    ins.then_inc(K["wt", p], 1)

            def weighted_sums(p, H):
                pe.wait_ge(K["sums_zeroed", p], p + 1)
                with pe.Fori(0, ITERS) as i:
                    for r in range(RING):
                        n = i * RING + r
                        pe.wait_ge(K["b_onehot_ready", p], n + 1)
                        pe.wait_ge(K["b_msg_ready", p], n + 1)
                        add_up(p, n, r, MS, D + H, K["b_free", p])
                nc.tensor.transpose(ps[:, 5, 0:P], ident[:, :], ident[:, :]).then_inc(K["sums_done", p], 1)

            logits_pass(4)
            relayout(4, HEADS)
            weighted_sums(4, HEADS)
            transposes("n4b", D, lambda b: C[:, b, 0:D], lambda g: 1)
            back("n4b", D, lambda a, b: CT[0:D, a:b], T["gelu", "n4b"])
            logits_pass(5)
            relayout(5, 1)
            weighted_sums(5, 1)

        @block.scalar
        def _(act):
            own = Own(act, own_act)

            def root():
                sqrt_no[0] += 1

            def sqrt_step(k, out_, in_):
                act.wait_ge(S["sqrt_in"], k)
                nc.scalar.activation(out_, in_, ACT.Sqrt).then_inc(S["sqrt_out"], 1)

            def read_tr(s_, rows_, dst):
                for g, (b0, nb) in enumerate(GROUPS):
                    act.wait_ge(T["tr", s_], g + 1 + gone("tr", s_))
                    nc.scalar.copy(dst[0:rows_, b0 * P:(b0 + nb) * P], ps[0:rows_, 4 + g % 2, 0:nb * P]).then_inc(T["tr_read", s_], 1)

            def read_mm(s_, rows_, dst, func, bias):
                for g, (b0, nb) in enumerate(GROUPS):
                    act.wait_ge(T["mm", s_], g + 1 + gone("mm", s_))
                    nc.scalar.activation(dst[0:rows_, b0 * P:(b0 + nb) * P], ps[0:rows_, 6 + g % 2, 0:nb * P], func,
                                         bias=bias).then_inc(T["mm_read", s_], 1)

            sqrt_step(1, st[:, 2, :], st[:, 1, :])
            for p in range(3):
                s_ = f"n{p}"
                read_tr(s_, P, CT)
                if p == 0:
                    act.wait_ge(S["weights_loaded"], 16 * 17)
                read_mm(s_, D, HT, ACT.Relu if p < 2 else ACT.Identity, bsage[:, p:p + 1])
            sqrt_step(2, st[:, 2, :], st[:, 1, :])
            with act.Fori(0, ITERS) as i:
                for r in range(RING):
                    n = i * RING + r
                    act.wait_ge(K["sum_ready3"], n + 1)
                    act.wait_ge(K["msg_free3"], n + 1)
                    nc.scalar.activation(MR[:, G * r:G * r + G, 0:D], MS[:, G * r:G * r + G, 0:D], ACT.Relu).then_inc(K["msg_ready3"], 1)
            read_tr("n3a", D, CT)
            read_mm("n3a", P, HT, ACT.Identity, v1s[:, 0:1])
            sqrt_step(3, bn[:, 2:3], bn[:, 1:2])
            act.wait_ge(bn_in, 1)
            for g, (b0, nb) in enumerate(GROUPS):
                ins = nc.scalar.activation(ZT[:, b0 * P:(b0 + nb) * P], HT[:, b0 * P:(b0 + nb) * P], ACT.Relu,
                                           bias=bn[:, 6:7], scale=bn[:, 5:6])
                if g == 0:
                    ins.then_inc(bn_out, 1)
                    act.wait_ge(bn_out, 1)
                    act.sem_inc(T["in_ready", "n3b"], 1)
                else:
                    ins.then_inc(T["in_ready", "n3b"], 1)
            act.wait_ge(T["in_ready", "n3b"], len(GROUPS))
            read_mm("n3b", D, HT, ACT.Identity, v2s[:, 0:1])
            sqrt_step(4, st[:, 2, :], st[:, 1, :])
            read_tr("n4a", D, HT)

            def logits_pass(p, k):
                act.sem_inc(K["store_free", p], RING)
                with act.Fori(0, ITERS) as i:
                    for r in range(RING):
                        n = i * RING + r
                        act.wait_ge(K["tr_ready", p], n + 1)
                        nc.scalar.copy(OT[:, r, :], ps[:, r, :]).then_inc(K["ot_ready", p], 1)
                        act.wait_ge(K["gathered", p, r], 16 * G * i + 16 * G + 16 * G * ITERS * p)
                        act.dma_start(gathered_d[k][:, bass.ds(n * G, G), :], GB[:, G * r:G * r + G, 0:D]).then_inc(K["xg_stored", p, r], 16)
                        if r:
                            act.wait_ge(K["xg_stored", p, r - 1], 16 * i + 16 + 16 * ITERS * (p - 4))
                            act.sem_inc(K["store_free", p], 1)
                    act.wait_ge(K["xg_stored", p, RING - 1], 16 * i + 16 + 16 * ITERS * (p - 4))
                    act.sem_inc(K["store_free", p], 1)

            def weigh(p, H):
                for h in range(H):
                    act.wait_ge(K["scan_done", p], h + 1)
                    nc.scalar.activation(FW[:, :], BW[:, :], ACT.Exp).then_inc(K["ex_done", p], 1)

            logits_pass(4, 0)
            weigh(4, HEADS)
            for g, (b0, nb) in enumerate(GROUPS):
                act.wait_ge(T["tr", "n4b"], g + 1 + gone("tr", "n4b"))
                nc.scalar.activation(ZT[0:D, b0 * P:(b0 + nb) * P], ps[0:D, 4 + g % 2, 0:nb * P], ACT.Identity,
                                     bias=v2s[:, 1:2]).then_inc(T["tr_read", "n4b"], 1)
            sqrt_step(5, bn[0:D, 2:3], bn[0:D, 1:2])
            act.wait_ge(bn_in, 2)
            for g, (b0, nb) in enumerate(GROUPS):
                sl = slice(b0 * P, (b0 + nb) * P)
                own(nc.scalar.activation(CT[0:D, sl], ZT[0:D, sl], ACT.Identity, bias=bn[0:D, 6:7], scale=bn[0:D, 5:6]))
                own.n += 0
                act.sem_inc(T["affine", "n4b"], 1)
            for g, (b0, nb) in enumerate(GROUPS):
                sl = slice(b0 * P, (b0 + nb) * P)
                act.wait_ge(bn_out, 2 + g)
                nc.scalar.activation(CT[0:D, sl], ZT[0:D, sl], ACT.Gelu).then_inc(T["gelu", "n4b"], 1)
            sqrt_step(6, st[:, 2, :], st[:, 1, :])
            logits_pass(5, 1)
            weigh(5, 1)

        @block.vector
        def _(dve):
            own = Own(dve, own_dve)
            V_ = nc.vector

            def bc(ap, shape):
                return ap.to_broadcast(shape)

            own(V_.memset(X[:, :, :], 0.0))
            V_.memset(LG[:, :, :], 0.0)
            V_.memset(XR[:, :, :], 0.0)
            V_.memset(AD[:, :], 0.0)
            V_.memset(AT[:, :], 1.0)
            V_.memset(GB[:, :, :], 1.0)
            V_.memset(ones[:, :], 1.0).then_inc(S["consts_set"], 1)
            dve.wait_ge(S["consts_set"], 1)
            dve.wait_ge(S["iota_made"], 1)
            own(V_.tensor_copy(iota_f[:, :], iota_i[:, :]))
            own(V_.tensor_copy(part_f[:, :], part_i[:, :]))
            own(V_.tensor_scalar(ident[:, :], iota_f[:, 0:P], part_f[:, 0:1], None, ALU.is_equal))
            dve.sem_inc(S["ident_made"], 1)

            dve.wait_ge(S["edges_loaded"], 32)
            own(V_.tensor_scalar(edge_i[0:1, :, :], edge_i[0:1, :, :], 7, None, ALU.arith_shift_right))
            own(V_.tensor_copy(edge_f[0:1, 0:2, :], edge_i[0:1, :, :]))
            own(V_.tensor_scalar(edge_f[0:1, 1, :], edge_f[0:1, 1, :], float(NB - 1), 1.0, ALU.min, ALU.add))
            own(V_.tensor_tensor(edge_f[0:1, 1, :], edge_f[0:1, 1, :], edge_f[0:1, 0, :], ALU.subtract))
            own(V_.memset(edge_f[0:1, 3, :], 0.0))
            own(V_.tensor_tensor_scan(edge_f[0:1, 2, :], edge_f[0:1, 1, :], edge_f[0:1, 3, :], 0.0, ALU.add, ALU.add))
            own(V_.tensor_tensor(edge_f[0:1, 3, :], edge_f[0:1, 1, :], edge_f[0:1, 2, :], ALU.subtract))
            V_.tensor_tensor(edge_f[0:1, 3, :], edge_f[0:1, 3, :], edge_f[0:1, 0, :], ALU.add).then_inc(S["edge_rows"], 1)
            dve.wait_ge(S["edge_bc"], 1)
            for k in range(2):
                for c in range(2):
                    a, b = c * 512, min(NT, c * 512 + 512)
                    ins = V_.tensor_copy(CD[:, k, a:b], ps[:, 2 * k + c, 0:b - a])
            ins.then_inc(S["cd_copied"], 1)
            dve.wait_ge(S["cd_copied"], 1)
            for j in range(QB):
                own(V_.tensor_scalar(wk[:, 0, :, :].rearrange("p a b -> p (a b)")[:, 0:NT], CD[:, 0, :], part_f[:, j:j + 1], 0.0,
                                     ALU.is_le, ALU.add, accum_out=pq[:, 0, j:j + 1]))
                own(V_.scalar_tensor_tensor(wk[:, 0, :, :].rearrange("p a b -> p (a b)")[:, 0:NT], iota_f[:, 0:NT], pq[:, 0, j:j + 1],
                                            CD[:, 1, :], ALU.is_equal, ALU.mult, accum_out=pq[:, 1, j:j + 1]))
            own(V_.tensor_tensor(pq[:, 2, :], pq[:, 1, :], part_f[:, :], ALU.add))
            own(V_.tensor_scalar(pq[:, 2, :], pq[:, 2, :], float(NB), None, ALU.min))
            own(V_.tensor_scalar(pq[:, 3, :], pq[:, 0, :], float(NT - 1), None, ALU.min))
            own(V_.tensor_scalar(pq[:, 4, :], pq[:, 2, :], float(PER_BANK), None, ALU.is_ge))
            own(V_.scalar_tensor_tensor(pq[:, 4, :], pq[:, 2, :], float(2 * PER_BANK), pq[:, 4, :], ALU.is_ge, ALU.add))
            own(V_.scalar_tensor_tensor(pq[:, 4, :], pq[:, 2, :], float(3 * PER_BANK), pq[:, 4, :], ALU.is_ge, ALU.add))
            own(V_.tensor_scalar(pq[:, 5, :], pq[:, 2, :], float(W), None, ALU.mult))
            own(V_.scalar_tensor_tensor(pq[:, 5, :], pq[:, 4, :], float(512 - PER_BANK * W), pq[:, 5, :], ALU.mult, ALU.add))
            own(V_.tensor_scalar(pq[:, 6, :], pq[:, 2, :], float(D), None, ALU.mult))
            own(V_.tensor_scalar(pq[:, 7, :], pq[:, 3, :], float(P), None, ALU.mult))
            own(V_.tensor_scalar(pq[:, 9, :], pq[:, 2, :], float(P), None, ALU.mult))
            own(V_.tensor_copy(pq[:, 8, :], pq[:, 2, :]))
            own(V_.tensor_copy(pqi[:, 0:4, :], pq[:, 5:9, :]))
            V_.tensor_copy(pqi[:, 4, :], pq[:, 3, :]).then_inc(S["pair_tile"], 1)
            dve.wait_ge(S["halo_gathered"], 32 * QB)
            own(V_.tensor_copy(hf[:, :, :], hg[:, :, :]))
            mid = hf[:, :, 1:P + 1]
            own(V_.tensor_tensor(wk[:, 4, :, :], mid, bc(pq[:, 9, :].unsqueeze(2), [P, QB, P]), ALU.subtract))
            own(V_.tensor_scalar(wk[:, 1, :, :], wk[:, 4, :, :], 0.0, None, ALU.is_ge))
            own(V_.scalar_tensor_tensor(wk[:, 0, :, :], wk[:, 4, :, :], float(P - 1), wk[:, 1, :, :], ALU.is_le, ALU.mult))
            own(V_.tensor_scalar(wk[:, 1, :, :], wk[:, 0, :, :], 1.0, BIG, ALU.subtract, ALU.mult))
            for f, nb_ in ((2, hf[:, :, 0:P]), (3, hf[:, :, 2:P + 2])):
                own(V_.tensor_tensor(wk[:, f, :, :], mid, nb_, ALU.not_equal))
                own(V_.scalar_tensor_tensor(wk[:, f, :, :], wk[:, f, :, :], -BIG, wk[:, 0, :, :], ALU.mult, ALU.mult))
            V_.tensor_copy(wk[:, 5, :, :], sg[:, :, :]).then_inc(S["flags_ready"], 1)
            for k in range(2):
                for j in range(QB):
                    n = k * QB + j
                    dve.wait_ge(S["pt"], n + 1)
                    V_.tensor_copy((dloc if k == 0 else src_i)[:, j * P:(j + 1) * P], ps[:, 4 + n % 4, 0:P]).then_inc(S["pt_copied"], 1)
            dve.wait_ge(S["pt_copied"], 2 * QB)

            def rsqrt_from(var, y, t, k):
                dve.wait_ge(S["sqrt_out"], k)
                own(V_.reciprocal(y, y))
                own(V_.tensor_tensor(t, y, y, ALU.mult))
                own(V_.tensor_tensor(t, t, var, ALU.mult))
                own(V_.tensor_scalar(t, t, -0.5, 1.5, ALU.mult, ALU.add))
                own(V_.tensor_tensor(y, y, t, ALU.mult))

            def layer_norm_relu(k):
                scr = HT[:, 0:NB * D].rearrange("p (b d) -> p b d", d=D)
                H = C[:, :, D:D2]
                own(V_.tensor_reduce(st[:, 0, :], X[:, :, :], AX_X, ALU.add))
                own(V_.tensor_scalar(st[:, 0, :], st[:, 0, :], 1.0 / D, None, ALU.mult))
                own(V_.tensor_tensor(H, X[:, :, :], bc(st[:, 0, :].unsqueeze(2), [P, NB, D]), ALU.subtract))
                own(V_.tensor_tensor(scr, H, H, ALU.mult))
                own(V_.tensor_reduce(st[:, 1, :], scr, AX_X, ALU.add))
                own(V_.tensor_scalar(st[:, 1, :], st[:, 1, :], 1.0 / D, EPS, ALU.mult, ALU.add))
                dve.sem_inc(S["sqrt_in"], 1)
                rsqrt_from(st[:, 1, :], st[:, 2, :], st[:, 3, :], k)
                own(V_.tensor_tensor(H, H, bc(st[:, 2, :].unsqueeze(2), [P, NB, D]), ALU.mult))
                own(V_.tensor_scalar(H, H, 0.0, None, ALU.max))

            def zero_sums(s):
                V_.memset(ps[:, 0:4, :], 0.0).then_inc(s, 1)

            def one_hot(n, r, free, ready, free_from=0):
                dve.wait_ge(free, n + 1 + free_from)
                V_.tensor_tensor(OH[:, G * r:G * r + G, :], bc(iota_f[:, 0:P].unsqueeze(1), [P, G, P]),
                                 bc(dloc[:, bass.ds(n * G, G)].unsqueeze(2), [P, G, P]), ALU.is_equal).then_inc(ready, 1)

            def batch_norm(rows_, zt, gamma, beta, k):
                b = bn[0:rows_, :]
                own(V_.tensor_reduce(b[:, 0:1], zt[0:rows_, 0:N], AX_X, ALU.add))
                own(V_.tensor_scalar(b[:, 0:1], b[:, 0:1], 1.0 / N, None, ALU.mult))
                own(V_.tensor_scalar(zt[0:rows_, :], zt[0:rows_, :], b[:, 0:1], None, ALU.subtract))
                own(V_.tensor_tensor(CT[0:rows_, 0:N], zt[0:rows_, 0:N], zt[0:rows_, 0:N], ALU.mult))
                own(V_.tensor_reduce(b[:, 1:2], CT[0:rows_, 0:N], AX_X, ALU.add))
                own(V_.tensor_scalar(b[:, 1:2], b[:, 1:2], 1.0 / N, EPS, ALU.mult, ALU.add))
                dve.sem_inc(S["sqrt_in"], 1)
                rsqrt_from(b[:, 1:2], b[:, 2:3], b[:, 3:4], k)
                own(V_.tensor_tensor(b[:, 5:6], b[:, 2:3], gamma, ALU.mult))
                own(V_.tensor_copy(b[:, 6:7], beta))
                dve.sem_inc(bn_in, 1)

            def finish_back(s_, add):
                for g, (b0, nb) in enumerate(GROUPS):
                    dve.wait_ge(T["bk", s_], g + 1 + gone("bk", s_))
                    src_ = ps[:, g % 2, 0:nb * D].rearrange("p (b d) -> p b d", d=D)
                    if add:
                        V_.tensor_tensor(X[:, b0:b0 + nb, :], X[:, b0:b0 + nb, :], src_, ALU.add).then_inc(T["bk_read", s_], 1)
                    else:
                        V_.tensor_copy(C[:, b0:b0 + nb, D:D2], src_).then_inc(T["bk_read", s_], 1)
                dve.wait_ge(T["bk_read", s_], len(GROUPS) + gone("bk", s_))

            dve.wait_ge(S["x_loaded"], 32)
            layer_norm_relu(1)
            dve.wait_ge(S["weights_loaded"], 16 * 17)
            for p in range(3):
                dve.sem_inc(K["table_ready", p], 1)
                zero_sums(K["sums_zeroed", p])
                dve.sem_inc(K["slot_free", p], RING)
                with dve.Fori(0, ITERS) as i:
                    for r in range(RING):
                        one_hot(i * RING + r, r, K["slot_free", p], K["onehot_ready", p], p * (RING + ITERS * RING))
                dve.wait_ge(K["sums_done", p], p + 1)
                if p == 0:
                    for k, b0, nb in BANKS:
                        own(V_.tensor_scalar(st[:, 4, b0:b0 + nb], acc_view(k, nb)[:, :, D], 1.0, None, ALU.max))
                    own(V_.reciprocal(st[:, 5, :], st[:, 4, :]))
                for k, b0, nb in BANKS:
                    own(V_.tensor_tensor(C[:, b0:b0 + nb, 0:D], acc_view(k, nb)[:, :, 0:D],
                                         bc(st[:, 5, b0:b0 + nb].unsqueeze(2), [P, nb, D]), ALU.mult))
                dve.sem_inc(T["in_ready", f"n{p}"], 1)
                finish_back(f"n{p}", p == 2)

            p = 3
            layer_norm_relu(2)
            dve.sem_inc(K["table_ready", p], 1)
            zero_sums(K["sums_zeroed", p])
            for s in (K["slot_free", p], K["onehot_free", p], K["attr_free3"], K["ef_free3"], K["msg_free3"]):
                dve.sem_inc(s, RING)
            with dve.Fori(0, ITERS) as i:
                for r in range(RING):
                    n = i * RING + r
                    one_hot(n, r, K["onehot_free", p], K["onehot_ready", p])
                    dve.wait_ge(K["gathered", p, r], 16 * G * i + 16 * G + 16 * G * ITERS * p)
                    dve.wait_ge(K["ef_ready3"], n + 1)
                    V_.tensor_tensor(MS[:, G * r:G * r + G, 0:D], GB[:, G * r:G * r + G, 0:D],
                                     ps[:, 4 + r, 0:G * D].rearrange("p (g d) -> p g d", d=D), ALU.add).then_inc(K["sum_ready3"], 1)
                    dve.wait_ge(K["sum_ready3"], n + 1)
                    dve.sem_inc(K["slot_free", p], 1)
                    dve.sem_inc(K["ef_free3"], 1)
                    dve.sem_inc(K["attr_free3"], 1)
                    dve.wait_ge(K["onehot_free", p], n + 1)
                    dve.sem_inc(K["msg_free3"], 1)
            dve.wait_ge(K["sums_done", p], p + 1)
            own(V_.tensor_scalar(eps_s[:, :], eps_s[:, :], 1.0, None, ALU.add))
            for k, b0, nb in BANKS:
                own(V_.scalar_tensor_tensor(C[:, b0:b0 + nb, 0:D], C[:, b0:b0 + nb, D:D2], eps_s[:, 0:1],
                                            acc_view(k, nb)[:, :, 0:D], ALU.mult, ALU.add))
            dve.sem_inc(T["in_ready", "n3a"], 1)
            dve.wait_ge(T["mm_read", "n3a"], len(GROUPS) + gone("mm", "n3a"))
            batch_norm(P, HT, v1s[:, 1:2], v1s[:, 2:3], 3)
            finish_back("n3b", True)

            layer_norm_relu(4)
            own(V_.memset(HT[D:D + 1, :], 1.0))
            dve.sem_inc(T["in_ready", "n4a"], 1)
            for g, (b0, nb) in enumerate(GROUPS):
                dve.wait_ge(T["mm", "n4a"], g + 1 + gone("mm", "n4a"))
                both = ps[:, 6 + g % 2, 0:nb * P].rearrange("p (b c) -> p b c", c=P)
                own(V_.tensor_copy(C[:, b0:b0 + nb, 0:D], both[:, :, 0:D]))
                V_.tensor_copy(XR[:, b0:b0 + nb, :], both[:, :, D:D2]).then_inc(T["mm_read", "n4a"], 1)
            dve.wait_ge(T["mm_read", "n4a"], len(GROUPS) + gone("mm", "n4a"))

            def credits(p):
                dve.sem_inc(K["slot_free", p], RING)

            def logits_pass(p):
                dve.sem_inc(K["table_ready", p], 1)
                credits(p)
                def hot(n, r):
                    one_hot(n, r, K["slot_free", p], K["onehot_ready", p], p * (RING + ITERS * RING))

                hot(0, 0)
                with dve.Fori(0, ITERS - 1) as i:
                    for r in range(RING):
                        hot(i * RING + r + 1, (r + 1) % RING)
                        logits(p, i, i * RING + r, r)
                for r in range(RING):
                    n = (ITERS - 1) * RING + r
                    if r + 1 < RING:
                        hot(n + 1, r + 1)
                    logits(p, ITERS - 1, n, r)
                dve.sem_inc(K["logits_done", p], 1)

            def logits(p, i, n, r):
                dve.wait_ge(K["gathered", p, r], 16 * G * i + 16 * G + 16 * G * ITERS * p)
                dve.wait_ge(K["g_ready", p], n + 1)
                rows_ = slice(G * r, G * r + G)
                m = 3 * n
                if p == 4:
                    V_.tensor_tensor(MS[:, rows_, 0:D], GB[:, rows_, 0:D],
                                     ps[:, 4 + r, 0:G * D].rearrange("p (g d) -> p g d", d=D), ALU.add).then_inc(K["own_loop", p], 1)
                    dve.wait_ge(K["own_loop", p], m + 1)
                    V_.scalar_tensor_tensor(MR[:, rows_, 0:D], MS[:, rows_, 0:D], 0.2, MS[:, rows_, 0:D], ALU.mult,
                                            ALU.max).then_inc(K["own_loop", p], 1)
                    dve.wait_ge(K["own_loop", p], m + 2)
                    V_.tensor_tensor(MS[:, rows_, 0:D], MR[:, rows_, 0:D], bc(att_s[:, :].unsqueeze(1), [P, G, D]),
                                     ALU.mult).then_inc(K["own_loop", p], 1)
                    dve.wait_ge(K["own_loop", p], m + 3)
                    V_.tensor_reduce(LG[:, bass.ds(n * G, G), :],
                                     MS[:, rows_, 0:D].rearrange("p g (h c) -> p g h c", h=HEADS), AX_X, ALU.add).then_inc(K["slot_free", p], 1)
                else:
                    V_.tensor_tensor(MS[:, rows_, 0:D], GB[:, rows_, 0:D], bc(attn_s[:, 0:D].unsqueeze(1), [P, G, D]),
                                     ALU.mult).then_inc(K["own_loop", p], 1)
                    dve.wait_ge(K["own_loop", p], m + 1)
                    V_.tensor_reduce(MR[:, rows_, 0], MS[:, rows_, 0:D], AX_X, ALU.add).then_inc(K["own_loop", p], 1)
                    dve.wait_ge(K["own_loop", p], m + 2)
                    V_.tensor_tensor(MR[:, rows_, 1], MR[:, rows_, 0], ps[:, 4 + r, 0:G], ALU.add).then_inc(K["own_loop", p], 1)
                    dve.wait_ge(K["own_loop", p], m + 3)
                    V_.scalar_tensor_tensor(LG[:, bass.ds(n * G, G), 0], MR[:, rows_, 1], 0.01, MR[:, rows_, 1], ALU.mult,
                                            ALU.max).then_inc(K["slot_free", p], 1)

            def softmax(p, H):
                for j in range(QB):
                    dve.wait_ge(K["lt", p], j + 1)
                    if j >= 2:
                        dve.wait_ge(K["lt_stored", p, j % 2], 16 * (j // 2))
                    V_.tensor_copy(tq[:, 0:H, (j % 2) * P:(j % 2 + 1) * P],
                                   ps[:, j % 2, 0:H * P].rearrange("p (h e) -> p h e", h=H)).then_inc(K["lt_copied", p], 1)
                if p == 4:
                    dve.wait_ge(S["flags_loaded"], 64)
                    for f in (2, 3):
                        own(V_.tensor_reduce(car[:, f:f + 1], flags[:, f, :], AX_X, ALU.min))
                own(V_.memset(crow[0:1, :, :], -BIG))
                n = 0
                for h in range(H):
                    dve.wait_ge(K["lt_loaded", p], 16 * h + 16)
                    own(V_.tensor_tensor(V[:, :], V[:, :], flags[:, 0, :], ALU.mult))
                    own(V_.tensor_tensor(V[:, :], V[:, :], flags[:, 1, :], ALU.add))
                    for d, buf in ((0, FW), (1, BW)):
                        step = slice(None, None, -1 if d else 1)
                        if d == 0 and h:
                            dve.wait_ge(K["wt_stored", p], 16 * h)
                        own(V_.tensor_tensor_scan(buf[:, step], flags[:, 2 + d, step], V[:, step], -BIG, ALU.add, ALU.max))
                        own(V_.tensor_copy(car[:, 0:1], buf[:, 0:1] if d else buf[:, NQ - 1:NQ]))
                        own(V_.tensor_copy(car[:, 1:2], car[:, 2 + d:3 + d]))
                        dve.sem_inc(K["carry_t", p], 1)
                        dve.wait_ge(K["carry_row", p], 2 * n + 1)
                        own(V_.tensor_copy(crow[0:1, 2:4, :], ps[0:1, 2, 0:2 * P].rearrange("p (a b) -> p a b", a=2)))
                        own(V_.tensor_tensor_scan(crow[0:1, 0, step], crow[0:1, 3, step], crow[0:1, 2, step], -BIG, ALU.add, ALU.max))
                        if d:
                            own(V_.memset(crow[0:1, 1, P - 1:P], -BIG))
                            own(V_.tensor_copy(crow[0:1, 1, 0:P - 1], crow[0:1, 0, 1:P]))
                        else:
                            own(V_.memset(crow[0:1, 1, 0:1], -BIG))
                            own(V_.tensor_copy(crow[0:1, 1, 1:P], crow[0:1, 0, 0:P - 1]))
                        dve.sem_inc(K["carry_back", p], 1)
                        dve.wait_ge(K["carry_row", p], 2 * n + 2)
                        own(V_.tensor_copy(car[:, 0:1], ps[:, 3, 0:1]))
                        dve.sem_inc(K["carry_back", p], 1)
                        own(V_.tensor_tensor_scan(buf[:, step], flags[:, 2 + d, step], V[:, step], car[:, 0:1], ALU.add, ALU.max))
                        n += 1
                    own(V_.tensor_tensor(FW[:, :], FW[:, :], BW[:, :], ALU.max))
                    own(V_.tensor_tensor(BW[:, :], V[:, :], FW[:, :], ALU.subtract))
                    dve.sem_inc(K["scan_done", p], 1)
                    dve.wait_ge(K["ex_done", p], h + 1)
                for j in range(QB):
                    m = min(P, NQ - j * P)
                    dve.wait_ge(K["wt", p], j + 1)
                    V_.tensor_copy(LG[:, j * P:j * P + m, 0:H].rearrange("p q h -> p h q"),
                                   ps[:, j % 2, 0:H * P].rearrange("p (h e) -> p h e", h=H)[:, :, 0:m]).then_inc(K["wt_copied", p], 1)
                dve.wait_ge(K["wt_copied", p], QB)

            def weighted_sums(p, H):
                zero_sums(K["sums_zeroed", p])
                dve.sem_inc(K["b_free", p], RING)
                with dve.Fori(0, ITERS) as i:
                    for r in range(RING):
                        n = i * RING + r
                        one_hot(n, r, K["b_free", p], K["b_onehot_ready", p])
                        dve.wait_ge(K["xg_loaded", p, r], 16 * i + 16 + 16 * ITERS * (p - 4))
                        rows_ = slice(G * r, G * r + G)
                        wts = LG[:, bass.ds(n * G, G), 0:H]
                        V_.tensor_copy(MS[:, rows_, D:D + H], wts)
                        V_.tensor_tensor(MS[:, rows_, 0:D].rearrange("p g (h c) -> p g h c", h=H),
                                         GB[:, rows_, 0:D].rearrange("p g (h c) -> p g h c", h=H),
                                         bc(wts.unsqueeze(3), [P, G, H, D // H]), ALU.mult).then_inc(K["b_msg_ready", p], 1)
                dve.wait_ge(K["sums_done", p], p + 1)

            logits_pass(4)
            softmax(4, HEADS)
            weighted_sums(4, HEADS)
            den = ZT[:, 0:NB * HEADS].rearrange("p (b h) -> p b h", h=HEADS)
            for k, b0, nb in BANKS:
                own(V_.tensor_scalar(den[:, b0:b0 + nb, :], acc_view(k, nb)[:, :, D:W], 1e-16, None, ALU.add))
            own(V_.reciprocal(den, den))
            for k, b0, nb in BANKS:
                for h in range(HEADS):
                    c = slice(h * D // HEADS, (h + 1) * D // HEADS)
                    own(V_.tensor_tensor(C[:, b0:b0 + nb, c], acc_view(k, nb)[:, :, c],
                                         bc(den[:, b0:b0 + nb, h].unsqueeze(2), [P, nb, D // HEADS]), ALU.mult))
            dve.sem_inc(T["in_ready", "n4b"], 1)
            dve.wait_ge(T["tr_read", "n4b"], len(GROUPS) + gone("tr", "n4b"))
            batch_norm(D, ZT, v2s[:, 2:3], v2s[:, 3:4], 5)
            for g, (b0, nb) in enumerate(GROUPS):
                sl = slice(b0 * P, (b0 + nb) * P)
                dve.wait_ge(T["affine", "n4b"], g + 1 )
                V_.tensor_tensor(ZT[0:D, sl], CT[0:D, sl], HT[0:D, sl], ALU.add).then_inc(bn_out, 1)
            finish_back("n4b", True)

            layer_norm_relu(6)
            scr = HT[:, 0:NB * D].rearrange("p (b d) -> p b d", d=D)
            own(V_.tensor_tensor(scr, C[:, :, D:D2], bc(attn_s[:, D:D2].unsqueeze(1), [P, NB, D]), ALU.mult))
            own(V_.tensor_reduce(AD[:, 0:NB], scr, AX_X, ALU.add))
            logits_pass(5)
            softmax(5, 1)
            weighted_sums(5, 1)
            for k, b0, nb in BANKS:
                own(V_.tensor_scalar(st[:, 4, b0:b0 + nb], acc_view(k, nb)[:, :, D], 1e-30, None, ALU.max))
            own(V_.reciprocal(st[:, 5, :], st[:, 4, :]))
            for k, b0, nb in BANKS:
                own(V_.tensor_tensor(C[:, b0:b0 + nb, 0:D], acc_view(k, nb)[:, :, 0:D],
                                     bc(st[:, 5, b0:b0 + nb].unsqueeze(2), [P, nb, D]), ALU.mult))
            own(V_.tensor_tensor(X[:, :, :], X[:, :, :], C[:, :, 0:D], ALU.add))
            dve.sem_inc(bn_in, 1)


def kernel(**inputs):
    import numpy as np
    import concourse.bacc as bacc
    from concourse import mybir as mb
    from concourse.bass_utils import run_bass_kernel_spmd

    v = {k: np.asarray(a) for k, a in inputs.items()}
    src_flat = np.zeros((NT * P,), np.int32)
    src_flat[:E] = v["src"]
    dst_flat = np.full((NT * P + 2,), NPAD + 895, np.int32)
    dst_flat[0] = -1
    dst_flat[1:E + 1] = v["dst"]
    attr_t = np.zeros((DE, NT * P), np.float32)
    attr_t[:, :E] = v["edge_attr_16"].T
    col = lambda a: np.ascontiguousarray(a.reshape(-1, 1))
    arrays = {
        "x": v["x"],
        "src_flat": src_flat,
        "dst_flat": dst_flat,
        "attr_t": attr_t,
        "w_sage": np.stack([np.concatenate([v[f"L0_gnn_W{k}l"].T, v[f"L0_gnn_W{k}r"].T], 0) for k in (1, 2, 3)]),
        "b_sage": np.stack([v[f"L0_gnn_b{k}"] for k in (1, 2, 3)], 1),
        "we1": np.concatenate([v["L1_gnn_W_e"].T, v["L1_gnn_b_e"][None]], 0),
        "w1t": v["L1_gnn_W1"].T, "b1": col(v["L1_gnn_b1"]), "gamma1": col(v["L1_gnn_gamma"]), "beta1": col(v["L1_gnn_beta"]),
        "eps1": v["L1_gnn_eps"], "w2t": v["L1_gnn_W2"].T, "b2": col(v["L1_gnn_b2"]),
        "wlr": np.concatenate([np.concatenate([v["L2_gnn_W_l"], v["L2_gnn_W_r"]], 1),
                               np.concatenate([v["L2_gnn_b_l"], v["L2_gnn_b_r"]])[None]], 0),
        "we2": v["L2_gnn_W_e"], "att": v["L2_gnn_att"].reshape(-1), "bias2": col(v["L2_gnn_bias"]),
        "gamma2": col(v["L2_gnn_gamma"]), "beta2": col(v["L2_gnn_beta"]), "attn": v["L3_gnn_attn_w"],
    }
    arrays = {f"in_{k}": np.ascontiguousarray(a) for k, a in arrays.items()}
    nc = bacc.Bacc("TRN2", target_bir_lowering=False, num_devices=1)
    args = [nc.dram_tensor(k, a.shape, mb.dt.from_np(a.dtype), kind="ExternalInput").ap() for k, a in arrays.items()]
    args.append(nc.dram_tensor("out_x", (N, D), F32, kind="ExternalOutput").ap())
    build(nc, *args)
    r = run_bass_kernel_spmd(nc, [arrays], core_ids=[0])
    return r.results[0]["out_x"]
```
